# Optimizing a Trainium2 kernel written in Bass

```python
import numpy as np
import jax
import jax.numpy as jnp

def _softmax(x, axis=-1):
    return jax.nn.softmax(x, axis=axis)
def _gelu(x):
    return jax.nn.gelu(x, approximate=True)
def _silu(x):
    return jax.nn.silu(x)
def _sigmoid(x):
    return jax.nn.sigmoid(x)
def _layernorm(x, axis=-1, eps=1e-5):
    m = jnp.mean(x, axis=axis, keepdims=True)
    v = jnp.var(x, axis=axis, keepdims=True)
    return (x - m) / jnp.sqrt(v + eps)
def _scatter_add(tgt, idx, src, axis=0):
    return tgt.at[idx].add(src)
def _segment_sum(src, seg, n):
    return jax.ops.segment_sum(src, seg, n)

kernel_name = 'mk_conv_preact_d1_conv_nchw32_f48b06'

def setup_inputs(seed: int = 0):
    np.random.seed(seed)
    _w = jnp.asarray
    def _rec_inputs():
        import jax
        import jax.numpy as jnp
        _gk = jax.random.key(seed)
        x = -9.26e-05 + 0.9999 * jax.random.normal(jax.random.fold_in(_gk, 1), (8, 32, 384, 384), jnp.float32)
        return x
    x = _rec_inputs()
    def _L0_conv_setup():
        import jax, jax.numpy as jnp
        import numpy as np
        B, C, H, W = (8, 32, 384, 384)
        PLANES, K, P, D, OFFSET = (32, 3, 1, 1, 1)

        def conv2d(x, w, b, pad, dil=1):
            out = jax.lax.conv_general_dilated(x, w, window_strides=(1, 1), padding=[(pad, pad), (pad, pad)], rhs_dilation=(dil, dil), dimension_numbers=('NCHW', 'OIHW', 'NCHW'))
            return out + b[None, :, None, None]

        def reflect(t, rng):
            two = 2.0 * rng
            m = jnp.mod(jnp.abs(t), two)
            r = jnp.where(m > rng, two - m, m)
            return jnp.clip(r, 0.0, rng)
        key = jax.random.key(seed)
        k1, k2, k3 = jax.random.split(key, 3)
        x = jax.random.normal(k1, (B, C, H, W), dtype=jnp.float32)
        koff = 2 * OFFSET + 1
        w_off = jax.random.normal(k2, (2 * C, C, koff, koff), dtype=jnp.float32) * (1.0 / np.sqrt(C * koff * koff))
        b_off = jnp.zeros((2 * C,), dtype=jnp.float32)
        w_dcn = jax.random.normal(k3, (PLANES, C, K, K), dtype=jnp.float32) * (1.0 / np.sqrt(C * K * K))
        b_dcn = jnp.zeros((PLANES,), dtype=jnp.float32)
        return {'x': x, 'w_off': w_off, 'b_off': b_off, 'w_dcn': w_dcn, 'b_dcn': b_dcn}
    _L0_conv_all = _L0_conv_setup()
    _L0_conv_in = {k: v for k, v in _L0_conv_all.items() if k in ('w_off', 'b_off', 'w_dcn', 'b_dcn', )}
    del _L0_conv_all

    return {
        "x": x,
        "L0_conv_w_off": _L0_conv_in["w_off"],
        "L0_conv_b_off": _L0_conv_in["b_off"],
        "L0_conv_w_dcn": _L0_conv_in["w_dcn"],
        "L0_conv_b_dcn": _L0_conv_in["b_dcn"],
    }

def reference(x, L0_conv_w_off, L0_conv_b_off, L0_conv_w_dcn, L0_conv_b_dcn):
    import jax
    import jax.numpy as jnp
    def _L0_conv_ref(x, w_off, b_off, w_dcn, b_dcn):
        import jax, jax.numpy as jnp
        import numpy as np
        B, C, H, W = (8, 32, 384, 384)
        PLANES, K, P, D, OFFSET = (32, 3, 1, 1, 1)

        def conv2d(x, w, b, pad, dil=1):
            out = jax.lax.conv_general_dilated(x, w, window_strides=(1, 1), padding=[(pad, pad), (pad, pad)], rhs_dilation=(dil, dil), dimension_numbers=('NCHW', 'OIHW', 'NCHW'))
            return out + b[None, :, None, None]

        def reflect(t, rng):
            two = 2.0 * rng
            m = jnp.mod(jnp.abs(t), two)
            r = jnp.where(m > rng, two - m, m)
            return jnp.clip(r, 0.0, rng)
        b, c, h, w = x.shape
        n = b * c
        off = (jax.nn.sigmoid(conv2d(x, w_off, b_off, OFFSET * D, D)) - 0.5) * (2.0 * OFFSET)
        off = off.reshape(n, 2, h, w)
        offx = off[:, 0] / (w - 1)
        offy = off[:, 1] / (h - 1)
        gy_base = jnp.arange(h, dtype=jnp.float32) / (h - 1) * 2.0 - 1.0
        gx_base = jnp.arange(w, dtype=jnp.float32) / (w - 1) * 2.0 - 1.0
        gx = gx_base[None, None, :] - offx
        gy = gy_base[None, :, None] - offy
        ix = reflect((gx + 1.0) * 0.5 * (w - 1), float(w - 1))
        iy = reflect((gy + 1.0) * 0.5 * (h - 1), float(h - 1))
        ix0 = jnp.floor(ix)
        iy0 = jnp.floor(iy)
        wx = ix - ix0
        wy = iy - iy0
        i0 = jnp.clip(ix0, 0, w - 1).astype(jnp.int32)
        i1 = jnp.clip(ix0 + 1, 0, w - 1).astype(jnp.int32)
        j0 = jnp.clip(iy0, 0, h - 1).astype(jnp.int32)
        j1 = jnp.clip(iy0 + 1, 0, h - 1).astype(jnp.int32)
        planes = x.reshape(n, h, w)
        nidx = jnp.arange(n)[:, None, None]
        v00 = planes[nidx, j0, i0]
        v01 = planes[nidx, j0, i1]
        v10 = planes[nidx, j1, i0]
        v11 = planes[nidx, j1, i1]
        sampled = v00 * (1 - wy) * (1 - wx) + v01 * (1 - wy) * wx + v10 * wy * (1 - wx) + v11 * wy * wx
        out = sampled.reshape(b, c, h, w)
        return conv2d(out, w_dcn, b_dcn, P, D)

    def _gn(v, G=16, eps=1e-5):
        B_, C_, H_, W_ = v.shape
        g = v.reshape(B_, G, C_ // G, H_, W_)
        m = jnp.mean(g, axis=(2, 3, 4), keepdims=True)
        s = jnp.var(g, axis=(2, 3, 4), keepdims=True)
        return ((g - m) / jnp.sqrt(s + eps)).reshape(v.shape)

    def _ln_c(v, eps=1e-6):
        m = jnp.mean(v, axis=1, keepdims=True)
        s = jnp.var(v, axis=1, keepdims=True)
        return (v - m) / jnp.sqrt(s + eps)

    def _ln_t(v, eps=1e-5):
        m = jnp.mean(v, axis=-1, keepdims=True)
        s = jnp.var(v, axis=-1, keepdims=True)
        return (v - m) / jnp.sqrt(s + eps)

    def _to_tokens(v):
        B_, C_, H_, W_ = v.shape
        return v.reshape(B_, C_, H_ * W_).transpose(0, 2, 1)
    def _from_tokens(t, like):
        B_, C_, H_, W_ = like.shape
        return t.transpose(0, 2, 1).reshape(B_, C_, H_, W_)

    x = x + _L0_conv_ref(_gn(x), L0_conv_w_off, L0_conv_b_off, L0_conv_w_dcn, L0_conv_b_dcn)
    return x


_drawn_inputs = setup_inputs


def setup_inputs(seed=0):
    import zlib

    import numpy as np

    out = dict(_drawn_inputs(seed))
    spreads = {'L0_conv_b_off': (0.0, 0.268), 'L0_conv_b_dcn': (0.0, 0.1)}
    factors = {}
    for name, (base, spread) in spreads.items():
        noise = np.random.default_rng([zlib.crc32(name.encode()), seed]).standard_normal(out[name].shape)
        drawn = base * np.exp(spread * noise) if base else spread * noise
        out[name] = jnp.asarray(drawn.astype(out[name].dtype))
    for name, factor in factors.items():
        out[name] = (out[name] * factor).astype(out[name].dtype)
    return out
```

```python
from contextlib import ExitStack

import concourse.bass as bass
from concourse import mybir

B, C, H, W = 8, 32, 384, 384
KW = 3
GROUP = 2
EPS = 1e-5

QR = 4
P = QR * C
G = 2
SR = G * QR
STEPS = H // SR
U = 6
ITERS = STEPS // U
WP = W + 2
HALF = P // 2

NX, NR, NN, NT, NU, NO = 6, 2, 3, 2, 2, 2
CREDIT = 6

BANDS = P // C
SPAN = H * W // BANDS
CH = 512
NCH = SPAN // CH
CPI = NCH // ITERS
PER_STEP = [0, 2, 2, 2, 2, 1]
assert sum(PER_STEP) == CPI and len(PER_STEP) == U and STEPS % U == 0 and NCH % ITERS == 0

OX, OY, OUTC = 0, 1, 2
CONSTS = 2 * KW + QR + 2
INNER, TOP, BOTTOM = 0, 1, 2


def conv_kernel(nc, x, w_all, bias_all, avg_src, avg_dst, out):
    f32 = mybir.dt.float32
    u32 = mybir.dt.uint32
    ALU = mybir.AluOpType
    ACT = mybir.ActivationFunctionType

    def rows(t, b, row0, step=QR):
        v = t[bass.ds(b, 1), :, :, :].rearrange("b c h w -> (b c) h w")
        return v[:, bass.ds(row0, G, step) if step != 1 else bass.ds(row0, G), :]

    xs = x.rearrange("b c (q r) w -> b (c q) (r w)", q=BANDS)

    ctx = ExitStack()
    with ctx:
        def sb(name, shape, dt=f32):
            return ctx.enter_context(nc.sbuf_tensor(name, shape, dt))

        def ps(name, shape):
            return ctx.enter_context(nc.psum_tensor(name, shape, f32))

        def sem(name):
            return ctx.enter_context(nc.semaphore(name))

        x0 = sb("x0", [P, NX, G, W])
        xn = sb("xn", [P, NR, 2, G, W])
        CENTRE, UP, MID, DOWN = 0, 1, 2, 3
        norm = sb("norm", [P, NN, 4, G, WP])
        near = sb("near", [P, NT, 3, G, WP])
        shift = sb("shift", [P, NT, 2, G, WP])
        pick = sb("pick", [P, NT, 2, G, WP])
        samp = sb("samp", [P, NU, G, WP])
        samp_up = sb("samp_up", [P, NU, G, WP])
        samp_dn = sb("samp_dn", [P, NU, G, WP])
        res = sb("res", [P, NO, G, W])
        stat_in = sb("stat_in", [P, 2, CPI * CH])
        stats = sb("stats", [P, NCH, 6])
        mv = sb("mv", [P, 2])
        dev = sb("dev", [P, 4])
        gvar = sb("gvar", [P, 1])
        minus_half = sb("minus_half", [P, 1])
        coef = sb("coef", [P, 2])
        wt = sb("wt", [P, 3, 3, KW, HALF])
        bias = sb("bias", [P, 3])
        a_src = sb("a_src", [P, P])
        a_dst = sb("a_dst", [P, P])

        p_off = [ps(f"p_off{k}", [P, G, 512]) for k in range(2)]
        p_out = ps("p_out", [P, G, 512])
        p_stat = ps("p_stat", [P, 512])

        consts_in = sem("consts_in")
        zeroed = sem("zeroed")
        weights_seq = sem("weights_seq")
        var_ready = sem("var_ready")
        root_done = sem("root_done")
        weights_ready = sem("weights_ready")
        pads_ready = sem("pads_ready")
        rows_in = [sem("rows_in_even"), sem("rows_in_odd")]
        moved = [sem("moved_even"), sem("moved_odd")]
        dn_last = [sem("dn_last_even"), sem("dn_last_odd")]
        stored = [sem("stored_even"), sem("stored_odd")]
        stat_got = [sem("stat_got_0"), sem("stat_got_1")]
        stat_seq = sem("stat_seq")
        stat_agg = sem("stat_agg")
        mean_mm = sem("mean_mm")
        dev_seq = sem("dev_seq")
        group_mm = sem("group_mm")
        coef_ready = sem("coef_ready")
        norm_done = sem("norm_done")
        near_pre = sem("near_pre")
        off_mm = [sem("xoff_mm"), sem("yoff_mm")]
        tanh_done = [sem("xtanh_done"), sem("ytanh_done")]
        size_done = [sem("xsize_done"), sem("ysize_done")]
        pick_done = [sem("xpick_done"), sem("ypick_done")]
        v_near = sem("v_near")
        v_centre = sem("v_centre")
        v_corner = sem("v_corner")
        v_xdiff = sem("v_xdiff")
        v_xprod = sem("v_xprod")
        v_xlerp = sem("v_xlerp")
        v_ydiff = sem("v_ydiff")
        v_yprod = sem("v_yprod")
        samp_done = sem("samp_done")
        out_mm = sem("out_mm")
        out_done = sem("out_done")

        held = {"sp": sem("sp_held"), "dve": sem("dve_held")}

        def hold(eng, name, semaphore, value):
            eng.wait_ge(semaphore, value)
            eng.sem_inc(held[name], 1)

        block = ctx.enter_context(nc.Block())

        ROWS_IN, MOVED, LAST, STORED = 3 * QR * 16, 5 * 16, 16, QR * 16

        def uses(b, i, u):
            return b * (STEPS // 2) + i * (U // 2) + u // 2 + 1

        def image(eng, step):
            with eng.Fori(0, B) as b:
                for u in range(U):
                    step(b, 0, u, u if u < 2 else None, u)
                with eng.Fori(1, ITERS - 1) as i:
                    for u in range(U):
                        step(b, i, i * U + u, None, u)
                for u in range(U):
                    s = STEPS - U + u
                    step(b, ITERS - 1, s, s if s >= STEPS - 2 else None, u)

        @block.sync
        def _(sp):
            sp.wait_ge(zeroed, 4)
            for ro in range(2):
                for ky in range(KW):
                    kr = ro + ky
                    sp.dma_start(
                        wt[kr * C:(kr + 1) * C, INNER, :, :, ro * C:(ro + 1) * C].rearrange("k u d m -> k (u d) m"),
                        w_all[ky].rearrange("u d k m -> k (u d) m")).then_inc(consts_in, 16)
            for r in range(QR):
                sp.dma_start(bias[r * C:(r + 1) * C, :], bias_all).then_inc(consts_in, 16)
            sp.dma_start(a_src[:, :], avg_src).then_inc(consts_in, 16)
            sp.dma_start(a_dst[:, :], avg_dst).then_inc(consts_in, 16)

            def load(b, row0, slot_x, slot_n, first, last):
                for r in range(QR):
                    sp.dma_start(x0[r * C:(r + 1) * C, slot_x], rows(x, b, row0 + r)).then_inc(rows_in[slot_n], 16)
                for r in range(QR):
                    src = rows(x, b, 1, QR - 2) if first and r == 0 else rows(x, b, row0 + r - 1)
                    sp.dma_start(xn[r * C:(r + 1) * C, slot_n, 0], src).then_inc(rows_in[slot_n], 16)
                for r in range(QR):
                    src = rows(x, b, H - QR, QR - 2) if last and r == QR - 1 else rows(x, b, row0 + r + 1)
                    sp.dma_start(xn[r * C:(r + 1) * C, slot_n, 1], src).then_inc(rows_in[slot_n], 16)

            for i in range(ITERS):
                if i >= 2:
                    sp.wait_ge(stat_seq, (i - 1) * CPI)
                sp.dma_start(stat_in[:, i % 2, :], xs[0, :, i * CPI * CH:(i + 1) * CPI * CH]).then_inc(stat_got[i % 2], 16)
            load(0, 0, 0, 0, True, False)
            load(0, SR, 1, 1, False, False)

            def step(b, i, m, s, u):
                n = b * STEPS + m
                nxt = (b + 1) % B
                if u == 0:
                    hold(sp, "sp", stat_seq, (b + 1) * NCH + i * CPI)
                    sp.dma_start(stat_in[:, 0, :],
                                 xs[bass.ds(nxt, 1), :, bass.ds(i * (CPI * CH), CPI * CH)].rearrange("b p f -> (b p) f")
                                 ).then_inc(stat_got[0], 16)
                hold(sp, "sp", out_done, n - 3 + CREDIT)
                hold(sp, "sp", norm_done, n + 1)
                edge = s is not None and s >= STEPS - 2
                bb, row = (nxt, (s + 2 - STEPS) * SR) if edge else (b, (m + 2) * SR)
                load(bb, row, (u + 2) % NX, u % NR, edge and row == 0,
                     isinstance(m, int) and m + 2 == STEPS - 1)
                hold(sp, "sp", samp_done, n + 1 + CREDIT)
                hold(sp, "sp", out_mm, n - 1 + CREDIT)
                a, z = u % NU, (u - 1) % NU
                sp.dma_start(samp_up[C:P, a], samp[0:P - C, a]).then_inc(moved[a], 16)
                sp.dma_start(samp_up[0:C, a, 1:G], samp[P - C:P, a, 0:G - 1]).then_inc(moved[a], 16)
                above = samp[P - C:P, a, G - 1] if s == 0 else samp[P - C:P, z, G - 1]
                if s == 0:
                    above = samp[0:C, a, 0]
                sp.dma_start(samp_up[0:C, a, 0], above).then_inc(moved[a], 16)
                sp.dma_start(samp_dn[0:P - C, a], samp[C:P, a]).then_inc(moved[a], 16)
                sp.dma_start(samp_dn[P - C:P, a, 0:G - 1], samp[0:C, a, 1:G]).then_inc(moved[a], 16)
                if s != 0:
                    sp.dma_start(samp_dn[P - C:P, z, G - 1], samp[0:C, a, 0]).then_inc(dn_last[z], 16)
                if s == STEPS - 1:
                    sp.dma_start(samp_dn[P - C:P, a, G - 1], samp[0:C, a, 0]).then_inc(dn_last[a], 16)

                def store(n, row0, u):
                    hold(sp, "sp", out_done, n + 1 + CREDIT)
                    for r in range(QR):
                        sp.dma_start(rows(out, b, row0 + r), res[r * C:(r + 1) * C, u % NO]).then_inc(stored[u % NO], 16)

                if s not in (0, 1):
                    store(n - 2, (m - 2) * SR, u)
                if s == STEPS - 1:
                    store(n - 1, (STEPS - 2) * SR, u - 1)
                    store(n, (STEPS - 1) * SR, u)

            for k in range(2):
                sp.sem_inc(moved[k], MOVED)
                sp.sem_inc(dn_last[k], LAST)
                sp.sem_inc(stored[k], STORED)
            image(sp, step)
            for k in range(2):
                sp.wait_ge(stored[k], (B * STEPS // 2 + 1) * STORED)
                sp.wait_ge(rows_in[k], (B * STEPS // 2 + 1) * ROWS_IN)

        @block.gpsimd
        def _(pool):
            for t in (norm, near, shift):
                nc.gpsimd.memset(t[:], 0.0).then_inc(pads_ready, 1)
            nc.gpsimd.memset(pick[:], 1.0).then_inc(pads_ready, 1)
            nc.gpsimd.memset(minus_half[:], -0.5).then_inc(pads_ready, 1)
            pool.wait_ge(pads_ready, 5)

            def root(images):
                pool.wait_ge(var_ready, images)
                nc.gpsimd.tensor_tensor(coef[:, 0:1], gvar[:, :], minus_half[:, :], ALU.pow).then_inc(root_done, 1)

            root(1)
            with pool.Fori(0, B) as b:
                root(b + 2)

        @block.scalar
        def _(act):
            act.wait_ge(pads_ready, 5)
            act.wait_ge(weights_ready, 2)

            def normalise(b, i, u):
                n, a = b * STEPS + i * U + u, u % NN
                act.wait_ge(rows_in[u % NR], uses(b, i, u) * ROWS_IN)
                act.wait_ge(samp_done, n - 2 + CREDIT)
                act.wait_ge(off_mm[1], n - 2 + CREDIT)
                nc.scalar.activation(norm[:, a, MID, :, 1:W + 1], x0[:, u % NX], ACT.Identity,
                                     bias=coef[:, 1:2], scale=coef[:, 0:1])
                for k, plane in ((0, UP), (1, DOWN)):
                    last = nc.scalar.activation(norm[:, a, plane, :, 1:W + 1], xn[:, u % NR, k], ACT.Identity,
                                                bias=coef[:, 1:2], scale=coef[:, 0:1])
                last.then_inc(norm_done, 1)

            def lay_out(n, u):
                a, t = u % NN, u % NT
                act.wait_ge(norm_done, n + 1)
                act.wait_ge(samp_done, n - 1 + CREDIT)
                for k, plane in enumerate((UP, MID, DOWN)):
                    nc.scalar.activation(near[:, t, k, :, 2:W + 1], norm[:, a, plane, :, 1:W], ACT.Copy)
                nc.scalar.activation(norm[:, a, CENTRE, :, 1:W + 1], norm[:, a, UP, :, 1:W + 1],
                                     ACT.Copy).then_inc(near_pre, 1)

            act.sem_inc(pick_done[0], CREDIT)
            act.sem_inc(pick_done[1], CREDIT)
            act.wait_ge(coef_ready, 1)
            normalise(0, 0, 0)
            lay_out(0, 0)

            def step(b, i, m, s, u):
                n = b * STEPS + m
                t = u % NT
                act.wait_ge(samp_done, n - 1 + CREDIT)
                for k in range(2):
                    lo = 1 if k == 0 else 0
                    act.wait_ge(off_mm[k], n + 1 + CREDIT)
                    nc.scalar.activation(shift[:, t, k, :, 1:W + 1], p_off[k][:, :, 0:W], ACT.Tanh,
                                         bias=bias[:, k:k + 1], scale=-0.5).then_inc(tanh_done[k], 1)
                    nc.scalar.activation(pick[:, t, k, :, 1 + lo:W + 1], p_off[k][:, :, lo:W], ACT.Relu,
                                         bias=bias[:, k:k + 1], scale=-0.5).then_inc(pick_done[k], 1)
                    act.wait_ge(tanh_done[k], n + 1)
                    nc.scalar.activation(shift[:, t, k, :, 1:W + 1], shift[:, t, k, :, 1:W + 1], ACT.Abs,
                                         scale=0.5).then_inc(size_done[k], 1)
                if s == STEPS - 1:
                    act.wait_ge(coef_ready, b + 2)
                normalise(b, i, u + 1)
                lay_out(n + 1, u + 1)

            image(act, step)

        @block.tensor
        def _(pe):
            pe.wait_ge(consts_in, 16 * CONSTS)
            pe.sem_inc(off_mm[0], CREDIT)
            pe.sem_inc(off_mm[1], CREDIT)
            pe.sem_inc(out_mm, CREDIT)

            def group_mean():
                nc.tensor.matmul(p_stat[:, 0:1], a_src[:, :], mv[:, 0:1], start=True, stop=True).then_inc(mean_mm, 1)

            def group_both():
                nc.tensor.matmul(p_stat[:, 2:4], a_dst[:, :], dev[:, 2:4], start=True, stop=True).then_inc(group_mm, 1)

            pe.wait_ge(stat_agg, 1)
            group_mean()
            pe.wait_ge(dev_seq, 3)
            group_both()
            pe.wait_ge(weights_ready, 2)

            def conv(dst, conv_no, above, below, first, last):
                for g in range(G):
                    for dx in range(KW):
                        for half, src in ((0, above), (1, below)):
                            v = TOP if first and g == 0 and half == 0 else \
                                BOTTOM if last and g == G - 1 and half == 1 else INNER
                            mm = nc.tensor.matmul(dst[half * HALF:(half + 1) * HALF, g, 0:W], wt[:, v, conv_no, dx, :],
                                                  src[:, g, dx:dx + W], start=(dx == 0), stop=(dx == KW - 1))
                return mm

            def offsets(n, u, first, last):
                a = u % NN
                pe.wait_ge(norm_done, n + 1)
                for k in range(2):
                    pe.wait_ge(pick_done[k], n + CREDIT)
                    conv(p_off[k], k, norm[:, a, UP], norm[:, a, DOWN], first, last).then_inc(off_mm[k], 1)

            def output(b, i, u, first, last):
                n, a = b * STEPS + i * U + u, u % NU
                pe.wait_ge(moved[a], (uses(b, i, u) + 1) * MOVED)
                pe.wait_ge(dn_last[a], (uses(b, i, u) + 1) * LAST)
                pe.wait_ge(out_done, n + CREDIT)
                conv(p_out, OUTC, samp_up[:, a], samp_dn[:, a], first, last).then_inc(out_mm, 1)

            def step(b, i, m, s, u):
                n = b * STEPS + m
                offsets(n, u, s == 0, s == STEPS - 1)
                if s == STEPS - 1:
                    pe.wait_ge(stat_agg, b + 2)
                    group_mean()
                if s not in (0, 1):
                    first_out = isinstance(m, int) and m == 2
                    output(b, i, u - 2, first_out, False)
                if s == STEPS - 1:
                    pe.wait_ge(dev_seq, (b + 2) * 3)
                    group_both()
                    output(b, i, u - 1, False, False)
                    output(b, i, u, False, True)

            image(pe, step)

        @block.vector
        def _(dve):
            nc.vector.memset(wt[:], 0.0).then_inc(zeroed, 1)
            nc.vector.memset(samp_up[:], 0.0).then_inc(zeroed, 1)
            nc.vector.memset(samp_dn[:], 0.0).then_inc(zeroed, 1)
            nc.vector.memset(samp[:], 0.0).then_inc(zeroed, 1)

            dve.wait_ge(consts_in, 16 * CONSTS)
            nc.vector.tensor_scalar(bias[:, 0:2], bias[:, 0:2], -0.5, None, ALU.mult).then_inc(weights_seq, 1)
            dve.wait_ge(weights_seq, 1)
            nc.vector.tensor_copy(wt[:, TOP], wt[:, INNER]).then_inc(weights_seq, 1)
            nc.vector.tensor_copy(wt[:, BOTTOM], wt[:, INNER]).then_inc(weights_seq, 1)
            dve.wait_ge(weights_seq, 3)
            nc.vector.memset(wt[0:C, TOP], 0.0).then_inc(weights_ready, 1)
            nc.vector.memset(wt[P - C:P, BOTTOM], 0.0).then_inc(weights_ready, 1)

            def bn(k, src):
                nc.vector.bn_stats(stats[:, k, :], src).then_inc(stat_seq, 1)

            def partition_stats(images):
                hold(dve, "dve", stat_seq, images * NCH)
                nc.vector.bn_aggr(mv[:, :], stats[:, :, :].rearrange("p k s -> p (k s)")).then_inc(stat_agg, 1)

            def deviation(images):
                dve.wait_ge(stat_agg, images)
                dve.wait_ge(mean_mm, images)
                nc.vector.tensor_tensor(dev[:, 0:1], mv[:, 0:1], p_stat[:, 0:1], ALU.subtract).then_inc(dev_seq, 1)
                nc.vector.tensor_copy(dev[:, 2:3], mv[:, 0:1]).then_inc(dev_seq, 1)
                dve.wait_ge(dev_seq, images * 3 - 1)
                nc.vector.scalar_tensor_tensor(dev[:, 3:4], dev[:, 0:1], dev[:, 0:1], mv[:, 1:2],
                                               ALU.mult, ALU.add).then_inc(dev_seq, 1)

            def coefficients(images, normalised):
                dve.wait_ge(group_mm, images)
                if normalised is not None:
                    dve.wait_ge(norm_done, normalised)
                nc.vector.tensor_scalar(gvar[:, :], p_stat[:, 3:4], EPS, None, ALU.add).then_inc(var_ready, 1)
                dve.wait_ge(root_done, images)
                nc.vector.scalar_tensor_tensor(coef[:, 1:2], p_stat[:, 2:3], -1.0, coef[:, 0:1],
                                               ALU.mult, ALU.mult).then_inc(coef_ready, 1)

            for k in range(NCH):
                if k % CPI == 0:
                    dve.wait_ge(stat_got[k // CPI % 2], (k // CPI // 2 + 1) * 16)
                bn(k, stat_in[:, k // CPI % 2, k % CPI * CH:(k % CPI + 1) * CH])
            partition_stats(1)
            deviation(1)
            coefficients(1, None)
            dve.sem_inc(samp_done, CREDIT)
            dve.sem_inc(out_done, CREDIT)

            def sample(b, i, u, first):
                n = b * STEPS + i * U + u
                a, t, z = u % NN, u % NT, u % NU
                hold(dve, "dve", near_pre, n + 1)
                hold(dve, "dve", pick_done[0], n + 1 + CREDIT)
                for k, plane in enumerate((UP, MID, DOWN)):
                    pk = nc.vector.copy_predicated(near[:, t, k, :, 1:W], pick[:, t, 0, :, 1:W].bitcast(u32),
                                                   norm[:, a, plane, :, 2:W + 1])
                pk.then_inc(v_near, 1)
                hold(dve, "dve", pick_done[1], n + 1 + CREDIT)
                nc.vector.copy_predicated(norm[:, a, CENTRE, :, 1:W + 1], pick[:, t, 1, :, 1:W + 1].bitcast(u32),
                                          norm[:, a, DOWN, :, 1:W + 1]).then_inc(v_centre, 1)
                hold(dve, "dve", v_near, n + 1)
                nc.vector.copy_predicated(near[:, t, 0, :, 1:W + 1], pick[:, t, 1, :, 1:W + 1].bitcast(u32),
                                          near[:, t, 2, :, 1:W + 1]).then_inc(v_corner, 1)
                base = norm[:, a, CENTRE:MID + 1:MID - CENTRE, :, :].rearrange("p k g w -> p k (g w)")
                pair = near[:, t, 0:2, :, :].rearrange("p k g w -> p k (g w)")
                tx = shift[:, t, 0:1].rearrange("p k g w -> p k (g w)").broadcast_to([P, 2, G * WP])
                ty = shift[:, t, 1].rearrange("p g w -> p (g w)")
                dve.wait_ge(v_corner, n + 1)
                dve.wait_ge(v_centre, n + 1)
                nc.vector.tensor_tensor(pair, pair, base, ALU.subtract).then_inc(v_xdiff, 1)
                dve.wait_ge(v_xdiff, n + 1)
                dve.wait_ge(size_done[0], n + 1)
                nc.vector.tensor_tensor(pair, tx, pair, ALU.mult).then_inc(v_xprod, 1)
                dve.wait_ge(v_xprod, n + 1)
                nc.vector.tensor_tensor(pair, base, pair, ALU.add).then_inc(v_xlerp, 1)
                chosen, middle = (near[:, t, k].rearrange("p g w -> p (g w)") for k in range(2))
                dve.wait_ge(v_xlerp, n + 1)
                nc.vector.tensor_tensor(chosen, chosen, middle, ALU.subtract).then_inc(v_ydiff, 1)
                dve.wait_ge(v_ydiff, n + 1)
                dve.wait_ge(size_done[1], n + 1)
                nc.vector.tensor_tensor(chosen, ty, chosen, ALU.mult).then_inc(v_yprod, 1)
                dve.wait_ge(v_yprod, n + 1)
                dve.wait_ge(moved[z], (uses(b, i, u - 2) + 1) * MOVED)
                dve.wait_ge(moved[1 - z], (uses(b, i, u - 1) + 1) * MOVED)
                if not first:
                    dve.wait_ge(dn_last[1 - z], (uses(b, i, u - 3) + 1) * LAST)
                nc.vector.tensor_tensor(samp[:, z].rearrange("p g w -> p (g w)"), middle, chosen, ALU.add).then_inc(samp_done, 1)

            def result(b, i, u):
                n = b * STEPS + i * U + u
                dve.wait_ge(out_mm, n + 1 + CREDIT)
                dve.wait_ge(stored[u % NO], (uses(b, i, u - 2) + 1) * STORED)
                nc.vector.scalar_tensor_tensor(res[:, u % NO], p_out[:, :, 0:W], bias[:, 2:3], x0[:, u % NX],
                                               ALU.add, ALU.add).then_inc(out_done, 1)

            def step(b, i, m, s, u):
                n = b * STEPS + m
                def some_stats():
                    first = sum(PER_STEP[:u])
                    for k in range(first, first + PER_STEP[u]):
                        if k == first:
                            dve.wait_ge(stat_got[0], (ITERS // 2 + b * ITERS + i + 1) * 16)
                        bn_at(i, k)

                def bn_at(i, k):
                    dst = stats[:, bass.ds(i * CPI + k, 1), :].rearrange("p k s -> p (k s)")
                    nc.vector.bn_stats(dst, stat_in[:, 0, k * CH:(k + 1) * CH]).then_inc(stat_seq, 1)

                if s == STEPS - 1:
                    some_stats()
                    partition_stats(b + 2)
                sample(b, i, u, s == 0)
                if s == STEPS - 1:
                    deviation(b + 2)
                else:
                    some_stats()
                if s not in (0, 1):
                    result(b, i, u - 2)
                if s == STEPS - 1:
                    coefficients(b + 2, (b + 1) * STEPS)
                    result(b, i, u - 1)
                    result(b, i, u)

            image(dve, step)


def kernel(x, L0_conv_w_off, L0_conv_b_off, L0_conv_w_dcn, L0_conv_b_dcn):
    import numpy as np
    import concourse.bacc as bacc
    from concourse.bass_utils import run_bass_kernel_spmd

    x, w_off, b_off, w_dcn, b_dcn = (np.ascontiguousarray(a) for a in (
        x, L0_conv_w_off, L0_conv_b_off, L0_conv_w_dcn, L0_conv_b_dcn))
    w_all = np.stack([w_off[0::2], w_off[1::2], w_dcn])
    w_all = np.ascontiguousarray(w_all.transpose(3, 0, 4, 2, 1))
    bias_all = np.ascontiguousarray(np.stack([b_off[0::2], b_off[1::2], b_dcn], axis=1))
    source = np.arange(P) // BANDS // GROUP
    target = np.arange(P) % C // GROUP
    share = np.float32(1 / (GROUP * BANDS))
    avg_src = np.where(source[:, None] == source[None, :], share, np.float32(0))
    avg_dst = np.where(source[:, None] == target[None, :], share, np.float32(0))

    nc = bacc.Bacc("TRN2", target_bir_lowering=False, num_devices=1)
    arrays = {"x": x, "w_all": w_all, "bias_all": bias_all, "avg_src": avg_src, "avg_dst": avg_dst}
    args = [nc.dram_tensor(f"in_{k}", a.shape, mybir.dt.from_np(a.dtype), kind="ExternalInput").ap()
            for k, a in arrays.items()]
    out = nc.dram_tensor("out", x.shape, mybir.dt.float32, kind="ExternalOutput").ap()
    conv_kernel(nc, *args, out)
    r = run_bass_kernel_spmd(nc, [{f"in_{k}": a for k, a in arrays.items()}], core_ids=[0])
    return r.results[0]["out"]
```

```python
from contextlib import ExitStack

import concourse.bass as bass
from concourse import mybir

B, C, H, W = 8, 32, 384, 384
KW = 3
GROUP = 2
EPS = 1e-5

QR = 4
P = QR * C
G = 2
SR = G * QR
STEPS = H // SR
U = 6
ITERS = STEPS // U
WP = W + 2
HALF = P // 2

AHEAD = 3
NX, NN, NT, NU, NO = 6, 3, 2, 3, 2
LAG = 3
CREDIT = 6

BANDS = P // C
SPAN = H * W // BANDS
CHUNKS = (ITERS - 2) * U
CH = SPAN // CHUNKS
NS = 2
assert CHUNKS * CH == SPAN and STEPS % U == 0 and CHUNKS % NS == 0

OX, OY, OUTC = 0, 1, 2
CONSTS = 2 * KW + QR + 2
INNER, TOP, BOTTOM = 0, 1, 2


def conv_kernel(nc, x, w_all, bias_all, avg_src, avg_dst, out):
    f32 = mybir.dt.float32
    u32 = mybir.dt.uint32
    ALU = mybir.AluOpType
    ACT = mybir.ActivationFunctionType

    def image(t, b):
        return t[bass.ds(b, 1), :, :, :].rearrange("b c h w -> (b c) h w")

    def own_rows(t, b, row0):
        return image(t, b)[:, bass.ds(row0, G, QR), :]

    def image_rows(b, row0, n):
        return image(x, b)[:, bass.ds(row0, n), :]

    def windows(b, row0):
        v = image(x, b)[:, bass.ds(row0 - 1, G, QR), :]
        return bass.AP(tensor=v.tensor, offset=v.offset, ap=[*v.ap[:-1], [1, 3 * W]])

    def chunks(b, q):
        v = x[bass.ds(b, 1), :, :, :].rearrange("b c (q r) w -> (b c q) (r w)", q=BANDS)
        return v[:, bass.ds(q * CH, CH)]

    ctx = ExitStack()
    with ctx:
        def sb(name, shape, dt=f32):
            return ctx.enter_context(nc.sbuf_tensor(name, shape, dt))

        def ps(name, shape):
            return ctx.enter_context(nc.psum_tensor(name, shape, f32))

        def sem(name):
            return ctx.enter_context(nc.semaphore(name))

        x_in = sb("x_in", [P, NX, G, 3, W])
        CENTRE, UP, MID, DOWN = 0, 1, 2, 3
        norm = sb("norm", [P, NN, 4, G, WP])
        near = sb("near", [P, NT, 3, G, WP])
        shift = sb("shift", [P, NT, 2, G, WP])
        pick = sb("pick", [P, NT, 2, G, WP])
        samp = sb("samp", [P, NU, G, WP])
        samp_up = sb("samp_up", [P, NU, G, WP])
        samp_dn = sb("samp_dn", [P, NU, G, WP])
        res = sb("res", [P, NO, G, W])
        stat_in = sb("stat_in", [P, NS, CH])
        stat_out = sb("stat_out", [P, CH])
        chunk_sum = sb("chunk_sum", [P, NS])
        neg_mean = sb("neg_mean", [P, CHUNKS])
        sq_dev = sb("sq_dev", [P, CHUNKS])
        bn_mean = sb("bn_mean", [P, 6])
        agg = sb("agg", [P, 3])
        mv = sb("mv", [P, 2])
        dev = sb("dev", [P, 4])
        gvar = sb("gvar", [P, 1])
        coef_next = sb("coef_next", [P, 2])
        minus_half = sb("minus_half", [P, 1])
        coef = sb("coef", [P, 2])
        wt = sb("wt", [P, 3, 3, KW, HALF])
        bias = sb("bias", [P, 3])
        a_src = sb("a_src", [P, P])
        a_dst = sb("a_dst", [P, P])

        p_off = [ps(f"p_off{k}", [P, G, 512]) for k in range(2)]
        p_out = ps("p_out", [P, G, 512])
        p_stat = ps("p_stat", [P, 512])

        consts_in = sem("consts_in")
        zeroed = sem("zeroed")
        weights_seq = sem("weights_seq")
        var_ready = sem("var_ready")
        root_done = sem("root_done")
        weights_ready = sem("weights_ready")
        pads_ready = sem("pads_ready")
        rows_in = [sem(f"rows_in_{k}") for k in range(AHEAD)]
        top_in = sem("top_in")
        bottom_in = sem("bottom_in")
        moved = [sem(f"moved_{k}") for k in range(NU)]
        dn_last = [sem(f"dn_last_{k}") for k in range(NU)]
        stored = [sem("stored_even"), sem("stored_odd")]
        stat_got = [sem("stat_got_0"), sem("stat_got_1")]
        sum_done = sem("sum_done")
        mean_done = sem("mean_done")
        stat_seq = sem("stat_seq")
        agg_seq = sem("agg_seq")
        stat_agg = sem("stat_agg")
        mean_mm = sem("mean_mm")
        dev_seq = sem("dev_seq")
        group_mm = sem("group_mm")
        coef_ready = sem("coef_ready")
        coef_set = sem("coef_set")
        norm_done = sem("norm_done")
        near_pre = sem("near_pre")
        off_mm = [sem("xoff_mm"), sem("yoff_mm")]
        tanh_done = [sem("xtanh_done"), sem("ytanh_done")]
        size_done = [sem("xsize_done"), sem("ysize_done")]
        pick_done = [sem("xpick_done"), sem("ypick_done")]
        v_near = sem("v_near")
        v_centre = sem("v_centre")
        v_corner = sem("v_corner")
        v_xdiff = sem("v_xdiff")
        v_xprod = sem("v_xprod")
        v_xlerp = sem("v_xlerp")
        v_ydiff = sem("v_ydiff")
        v_yprod = sem("v_yprod")
        samp_done = sem("samp_done")
        out_mm = sem("out_mm")
        out_done = sem("out_done")

        held = {"sp": sem("sp_held"), "dve": sem("dve_held")}

        def hold(eng, name, semaphore, value):
            eng.wait_ge(semaphore, value)
            eng.sem_inc(held[name], 1)

        block = ctx.enter_context(nc.Block())

        def flat(planes):
            return planes.rearrange("p k g w -> p k (g w)")

        ROWS_IN, EDGE_IN, MOVED, LAST, STORED = QR * 16, 2 * 16, 5 * 16, 16, QR * 16

        def uses(b, i, u, ring):
            return b * (STEPS // ring) + i * (U // ring) + u // ring + 1

        def images(eng, step):
            def one(b, fresh):
                for u in range(U):
                    step(b, 0, u, u, fresh)
                with eng.Fori(1, ITERS - 1) as i:
                    for u in range(U):
                        step(b, i, u, None, False)
                for u in range(U):
                    step(b, ITERS - 1, u, STEPS - U + u, False)

            one(0, True)
            with eng.Fori(1, B) as b:
                one(b, False)

        def stat_load(eng, b, q, slot):
            eng.dma_start(stat_in[:, slot, :], chunks(b, q)).then_inc(stat_got[slot], 16)

        @block.sync
        def _(sp):
            sp.wait_ge(zeroed, 4)
            for ro in range(2):
                for ky in range(KW):
                    kr = ro + ky
                    sp.dma_start(
                        wt[kr * C:(kr + 1) * C, INNER, :, :, ro * C:(ro + 1) * C].rearrange("k u d m -> k (u d) m"),
                        w_all[ky].rearrange("u d k m -> k (u d) m")).then_inc(consts_in, 16)
            for r in range(QR):
                sp.dma_start(bias[r * C:(r + 1) * C, :], bias_all).then_inc(consts_in, 16)
            sp.dma_start(a_src[:, :], avg_src).then_inc(consts_in, 16)
            sp.dma_start(a_dst[:, :], avg_dst).then_inc(consts_in, 16)

            def load(b, row0, slot, first, last):
                landed = rows_in[slot % AHEAD]
                for r in range(QR):
                    dst = x_in[r * C:(r + 1) * C, slot]
                    if first and r == 0:
                        sp.dma_start(dst[:, 1], image_rows(b, QR - 1, 3)).then_inc(landed, 16)
                        sp.dma_start(dst[:, 0, 1:3], image_rows(b, 0, 2)).then_inc(top_in, 16)
                        sp.dma_start(dst[:, 0, 0:1], image_rows(b, 1, 1)).then_inc(top_in, 16)
                    elif last and r == QR - 1:
                        sp.dma_start(dst[:, 0], image_rows(b, H - QR - 2, 3)).then_inc(landed, 16)
                        sp.dma_start(dst[:, 1, 0:2], image_rows(b, H - 2, 2)).then_inc(bottom_in, 16)
                        sp.dma_start(dst[:, 1, 2:3], image_rows(b, H - 2, 1)).then_inc(bottom_in, 16)
                    else:
                        sp.dma_start(dst.rearrange("c g k w -> c g (k w)"), windows(b, row0 + r)).then_inc(landed, 16)

            for q in range(CHUNKS):
                if q >= NS:
                    sp.wait_ge(stat_seq, q - NS + 1)
                stat_load(sp, 0, q, q % NS)
            for s in range(AHEAD):
                load(0, s * SR, s, s == 0, False)

            def step(b, i, u, s, fresh):
                m = i * U + u
                n = b * STEPS + m
                nxt = (b + 1) % B
                hold(sp, "sp", out_done, n + AHEAD - NX + 1 + CREDIT)
                hold(sp, "sp", norm_done, n + 1)
                over = s is not None and s >= STEPS - AHEAD
                bb, row = (nxt, (s + AHEAD - STEPS) * SR) if over else (b, (m + AHEAD) * SR)
                load(bb, row, (u + AHEAD) % NX, over and row == 0, s == STEPS - 1 - AHEAD)
                hold(sp, "sp", samp_done, n + 1 + CREDIT)
                hold(sp, "sp", out_mm, n - LAG + 1 + CREDIT)
                a, z = u % NU, (u - 1) % NU
                sp.dma_start(samp_up[C:P, a], samp[0:P - C, a]).then_inc(moved[a], 16)
                sp.dma_start(samp_up[0:C, a, 1:G], samp[P - C:P, a, 0:G - 1]).then_inc(moved[a], 16)
                above = samp[P - C:P, a, G - 1] if s == 0 else samp[P - C:P, z, G - 1]
                if s == 0:
                    above = samp[0:C, a, 0]
                sp.dma_start(samp_up[0:C, a, 0], above).then_inc(moved[a], 16)
                sp.dma_start(samp_dn[0:P - C, a], samp[C:P, a]).then_inc(moved[a], 16)
                sp.dma_start(samp_dn[P - C:P, a, 0:G - 1], samp[0:C, a, 1:G]).then_inc(moved[a], 16)
                if s != 0:
                    sp.dma_start(samp_dn[P - C:P, z, G - 1], samp[0:C, a, 0]).then_inc(dn_last[z], 16)
                if s == STEPS - 1:
                    sp.dma_start(samp_dn[P - C:P, a, G - 1], samp[0:C, a, 0]).then_inc(dn_last[a], 16)

                if not (fresh and s < LAG):
                    before = s is not None and s < LAG
                    store(n - LAG, b - 1 if before else b, (STEPS + s - LAG if before else m - LAG) * SR, u - LAG)

            def store(n, b, row0, u):
                hold(sp, "sp", out_done, n + 1 + CREDIT)
                for r in range(QR):
                    sp.dma_start(own_rows(out, b, row0 + r), res[r * C:(r + 1) * C, u % NO]).then_inc(stored[u % NO], 16)

            for k in range(NU):
                sp.sem_inc(moved[k], MOVED)
                sp.sem_inc(dn_last[k], LAST)
            for k in range(NO):
                sp.sem_inc(stored[k], STORED)
            images(sp, step)
            for late in range(LAG):
                s = STEPS - LAG + late
                store((B - 1) * STEPS + s, B - 1, s * SR, s)
            for k in range(2):
                sp.wait_ge(stored[k], (B * STEPS // 2 + 1) * STORED)
            for k in range(AHEAD):
                sp.wait_ge(rows_in[k], (B * STEPS // AHEAD + 1) * ROWS_IN)

        @block.gpsimd
        def _(pool):
            for t in (norm, near, shift):
                nc.gpsimd.memset(t[:], 0.0).then_inc(pads_ready, 1)
            nc.gpsimd.memset(pick[:], 0.0).then_inc(pads_ready, 1)
            pool.wait_ge(pads_ready, 4)
            nc.gpsimd.memset(pick[:, :, 0, :, 1:2], 1.0).then_inc(pads_ready, 1)
            nc.gpsimd.memset(minus_half[:], -0.5).then_inc(pads_ready, 1)
            pool.wait_ge(pads_ready, 6)

            def root(images):
                pool.wait_ge(var_ready, images)
                nc.gpsimd.tensor_tensor(coef_next[:, 0:1], gvar[:, :], minus_half[:, :], ALU.pow).then_inc(root_done, 1)

            root(1)
            with pool.Fori(0, B) as b:
                root(b + 2)

        @block.scalar
        def _(act):
            act.wait_ge(pads_ready, 6)
            act.wait_ge(weights_ready, 2)

            def normalise(b, i, u, s):
                n, a = b * STEPS + i * U + u, u % NN
                act.wait_ge(rows_in[u % AHEAD], uses(b, i, u, AHEAD) * ROWS_IN)
                if s is not None and s % STEPS == 0:
                    act.wait_ge(top_in, (b + 1 + s // STEPS) * EDGE_IN)
                if s == STEPS - 1:
                    act.wait_ge(bottom_in, (b + 1) * EDGE_IN)
                act.wait_ge(samp_done, n - 2 + CREDIT)
                act.wait_ge(off_mm[1], n - 2 + CREDIT)
                nc.scalar.activation(norm[:, a, UP:DOWN + 1, :, 1:W + 1], x_in[:, u % NX].rearrange("p g k w -> p k g w"),
                                     ACT.Identity, bias=coef[:, 1:2], scale=coef[:, 0:1]).then_inc(norm_done, 1)

            def lay_out(n, u):
                a, t = u % NN, u % NT
                act.wait_ge(norm_done, n + 1)
                act.wait_ge(samp_done, n - 1 + CREDIT)
                nc.scalar.activation(flat(near[:, t])[:, :, 1:G * WP],
                                     flat(norm[:, a, UP:DOWN + 1])[:, :, 0:G * WP - 1], ACT.Copy)
                nc.scalar.activation(norm[:, a, CENTRE, :, 1:W + 1], norm[:, a, UP, :, 1:W + 1],
                                     ACT.Copy).then_inc(near_pre, 1)

            act.sem_inc(pick_done[0], CREDIT)
            act.sem_inc(pick_done[1], CREDIT)
            def new_coefficients(images):
                act.wait_ge(coef_ready, images)
                act.wait_ge(norm_done, (images - 1) * STEPS)
                nc.scalar.activation(coef[:, :], coef_next[:, :], ACT.Copy).then_inc(coef_set, 1)
                act.wait_ge(coef_set, images)

            def chunk_stats(images, q, slot, n_got):
                act.wait_ge(stat_got[slot], n_got * 16)
                act.wait_ge(stat_seq, images * CHUNKS + q)
                nc.scalar.activation(stat_out[:, :], stat_in[:, slot, :], ACT.Copy,
                                     accum_out=chunk_sum[:, slot:slot + 1]).then_inc(sum_done, 1)
                act.wait_ge(sum_done, images * CHUNKS + q + 1)
                mean = neg_mean[:, bass.ds(q, 1)]
                nc.scalar.activation(neg_mean[:, bass.ds(q, 1)], chunk_sum[:, slot:slot + 1], ACT.Copy,
                                     scale=-1.0 / CH).then_inc(mean_done, 1)
                act.wait_ge(mean_done, images * CHUNKS + q + 1)
                nc.scalar.activation(stat_out[:, :], stat_in[:, slot, :], ACT.Square, bias=mean,
                                     accum_out=sq_dev[:, bass.ds(q, 1)]).then_inc(stat_seq, 1)

            for q in range(CHUNKS):
                chunk_stats(0, q, q % NS, q // NS + 1)
            act.wait_ge(coef_ready, 1)
            nc.scalar.activation(coef[:, :], coef_next[:, :], ACT.Copy).then_inc(coef_set, 1)
            act.wait_ge(coef_set, 1)
            normalise(0, 0, 0, 0)
            lay_out(0, 0)

            def step(b, i, u, s, fresh):
                m = i * U + u
                n = b * STEPS + m
                t = u % NT
                if s is None:
                    q = (i - 1) * U + u
                    act.wait_ge(stat_seq, (b + 1) * CHUNKS + q - NS + 1)
                    stat_load(act, (b + 1) % B, q, u % NS)
                act.wait_ge(samp_done, n - 1 + CREDIT)
                for k in range(2):
                    lo, hi = (1, W - 1) if k == 0 else (0, W)
                    act.wait_ge(off_mm[k], n + 1 + CREDIT)
                    nc.scalar.activation(shift[:, t, k, :, 1:W + 1], p_off[k][:, :, 0:W], ACT.Tanh,
                                         bias=bias[:, k:k + 1], scale=-0.5).then_inc(tanh_done[k], 1)
                    nc.scalar.activation(pick[:, t, k, :, 1 + lo:1 + hi], p_off[k][:, :, lo:hi], ACT.Relu,
                                         bias=bias[:, k:k + 1], scale=-0.5).then_inc(pick_done[k], 1)
                    act.wait_ge(tanh_done[k], n + 1)
                    nc.scalar.activation(shift[:, t, k, :, 1:W + 1], shift[:, t, k, :, 1:W + 1], ACT.Abs,
                                         scale=0.5).then_inc(size_done[k], 1)
                    if k == 0:
                        if s == STEPS - 1:
                            new_coefficients(b + 2)
                        normalise(b, i, u + 1, None if s is None else s + 1)
                lay_out(n + 1, u + 1)
                if s is None:
                    chunk_stats(b + 1, q, u % NS, (b + 1) * (CHUNKS // NS) + (i - 1) * (U // NS) + u // NS + 1)

            images(act, step)

        @block.tensor
        def _(pe):
            pe.wait_ge(consts_in, 16 * CONSTS)
            pe.sem_inc(off_mm[0], CREDIT)
            pe.sem_inc(off_mm[1], CREDIT)
            pe.sem_inc(out_mm, CREDIT)

            def group_mean():
                nc.tensor.matmul(p_stat[:, 0:1], a_src[:, :], mv[:, 0:1], start=True, stop=True).then_inc(mean_mm, 1)

            def group_both():
                nc.tensor.matmul(p_stat[:, 2:4], a_dst[:, :], dev[:, 2:4], start=True, stop=True).then_inc(group_mm, 1)

            pe.wait_ge(stat_agg, 1)
            pe.wait_ge(agg_seq, 4)
            group_mean()
            pe.wait_ge(dev_seq, 3)
            group_both()
            pe.wait_ge(weights_ready, 2)

            def conv(dst, conv_no, above, below, first, last):
                for g in range(G):
                    for dx in range(KW):
                        for half, src in ((0, above), (1, below)):
                            v = TOP if first and g == 0 and half == 0 else \
                                BOTTOM if last and g == G - 1 and half == 1 else INNER
                            mm = nc.tensor.matmul(dst[half * HALF:(half + 1) * HALF, g, 0:W], wt[:, v, conv_no, dx, :],
                                                  src[:, g, dx:dx + W], start=(dx == 0), stop=(dx == KW - 1))
                return mm

            def offsets(n, u, first, last):
                a = u % NN
                pe.wait_ge(norm_done, n + 1)
                for k in range(2):
                    pe.wait_ge(pick_done[k], n + CREDIT)
                    conv(p_off[k], k, norm[:, a, UP], norm[:, a, DOWN], first, last).then_inc(off_mm[k], 1)

            def output(b, i, u, first, last):
                n, a = b * STEPS + i * U + u, u % NU
                pe.wait_ge(moved[a], (uses(b, i, u, NU) + 1) * MOVED)
                pe.wait_ge(dn_last[a], (uses(b, i, u, NU) + 1) * LAST)
                pe.wait_ge(out_done, n + CREDIT)
                conv(p_out, OUTC, samp_up[:, a], samp_dn[:, a], first, last).then_inc(out_mm, 1)

            def step(b, i, u, s, fresh):
                m = i * U + u
                n = b * STEPS + m
                if s == STEPS - 2:
                    pe.wait_ge(dev_seq, (b + 2) * 3)
                    group_both()
                offsets(n, u, s == 0, s == STEPS - 1)
                if s == STEPS - 3:
                    pe.wait_ge(stat_agg, b + 2)
                    pe.wait_ge(agg_seq, (b + 2) * 4)
                    group_mean()
                if not (fresh and s < LAG):
                    output(b, i, u - LAG, s == LAG, s == LAG - 1)

            images(pe, step)
            for late in range(U - LAG, U):
                output(B - 1, ITERS - 1, late, False, late == U - 1)

        @block.vector
        def _(dve):
            nc.vector.memset(wt[:], 0.0).then_inc(zeroed, 1)
            nc.vector.memset(samp_up[:], 0.0).then_inc(zeroed, 1)
            nc.vector.memset(samp_dn[:], 0.0).then_inc(zeroed, 1)
            nc.vector.memset(samp[:], 0.0).then_inc(zeroed, 1)

            dve.wait_ge(consts_in, 16 * CONSTS)
            nc.vector.tensor_scalar(bias[:, 0:2], bias[:, 0:2], -0.5, None, ALU.mult).then_inc(weights_seq, 1)
            dve.wait_ge(weights_seq, 1)
            nc.vector.tensor_copy(wt[:, TOP], wt[:, INNER]).then_inc(weights_seq, 1)
            nc.vector.tensor_copy(wt[:, BOTTOM], wt[:, INNER]).then_inc(weights_seq, 1)
            dve.wait_ge(weights_seq, 3)
            nc.vector.memset(wt[0:C, TOP], 0.0).then_inc(weights_ready, 1)
            nc.vector.memset(wt[P - C:P, BOTTOM], 0.0).then_inc(weights_ready, 1)

            def partition_stats(images):
                dve.wait_ge(stat_seq, images * CHUNKS)
                nc.vector.bn_stats(bn_mean[:, :], neg_mean[:, :]).then_inc(agg_seq, 1)
                nc.vector.reduce_sum(agg[:, 2:3], sq_dev[:, :], axis=mybir.AxisListType.X).then_inc(agg_seq, 1)
                hold(dve, "dve", agg_seq, images * 4 - 2)
                nc.vector.bn_aggr(agg[:, 0:2], bn_mean[:, :]).then_inc(agg_seq, 1)
                dve.wait_ge(agg_seq, images * 4 - 1)
                nc.vector.tensor_scalar(mv[:, 0:1], agg[:, 0:1], -1.0, None, ALU.mult).then_inc(agg_seq, 1)
                nc.vector.scalar_tensor_tensor(mv[:, 1:2], agg[:, 2:3], 1.0 / SPAN, agg[:, 1:2],
                                               ALU.mult, ALU.add).then_inc(stat_agg, 1)

            def deviation(images):
                dve.wait_ge(stat_agg, images)
                dve.wait_ge(agg_seq, images * 4)
                dve.wait_ge(mean_mm, images)
                nc.vector.tensor_tensor(dev[:, 0:1], mv[:, 0:1], p_stat[:, 0:1], ALU.subtract).then_inc(dev_seq, 1)
                nc.vector.tensor_copy(dev[:, 2:3], mv[:, 0:1]).then_inc(dev_seq, 1)
                dve.wait_ge(dev_seq, images * 3 - 1)
                nc.vector.scalar_tensor_tensor(dev[:, 3:4], dev[:, 0:1], dev[:, 0:1], mv[:, 1:2],
                                               ALU.mult, ALU.add).then_inc(dev_seq, 1)

            def variance(images):
                dve.wait_ge(group_mm, images)
                nc.vector.tensor_scalar(gvar[:, :], p_stat[:, 3:4], EPS, None, ALU.add).then_inc(var_ready, 1)

            def coefficients(images):
                dve.wait_ge(root_done, images)
                nc.vector.scalar_tensor_tensor(coef_next[:, 1:2], p_stat[:, 2:3], -1.0, coef_next[:, 0:1],
                                               ALU.mult, ALU.mult).then_inc(coef_ready, 1)

            partition_stats(1)
            deviation(1)
            variance(1)
            coefficients(1)
            dve.sem_inc(samp_done, CREDIT)
            dve.sem_inc(out_done, CREDIT)

            def result(b, i, u):
                n = b * STEPS + i * U + u
                dve.wait_ge(out_mm, n + 1 + CREDIT)
                dve.wait_ge(stored[u % NO], (uses(b, i, u - 2, NO) + 1) * STORED)
                nc.vector.scalar_tensor_tensor(res[:, u % NO], p_out[:, :, 0:W], bias[:, 2:3], x_in[:, u % NX, :, 1],
                                               ALU.add, ALU.add).then_inc(out_done, 1)

            def sample(b, i, u, fresh):
                n = b * STEPS + i * U + u
                a, t, z = u % NN, u % NT, u % NU
                hold(dve, "dve", near_pre, n + 1)
                hold(dve, "dve", pick_done[0], n + 1 + CREDIT)
                nc.vector.copy_predicated(
                    flat(near[:, t])[:, :, 0:G * WP - 1],
                    flat(pick[:, t, 0:1]).bitcast(u32)[:, :, 0:G * WP - 1].broadcast_to([P, 3, G * WP - 1]),
                    flat(norm[:, a, UP:DOWN + 1])[:, :, 1:G * WP]).then_inc(v_near, 1)
                hold(dve, "dve", pick_done[1], n + 1 + CREDIT)
                nc.vector.copy_predicated(norm[:, a, CENTRE, :, 1:W + 1], pick[:, t, 1, :, 1:W + 1].bitcast(u32),
                                          norm[:, a, DOWN, :, 1:W + 1]).then_inc(v_centre, 1)
                hold(dve, "dve", v_near, n + 1)
                nc.vector.copy_predicated(near[:, t, 0, :, 1:W + 1], pick[:, t, 1, :, 1:W + 1].bitcast(u32),
                                          near[:, t, 2, :, 1:W + 1]).then_inc(v_corner, 1)
                base = norm[:, a, CENTRE:MID + 1:MID - CENTRE, :, :].rearrange("p k g w -> p k (g w)")
                pair = near[:, t, 0:2, :, :].rearrange("p k g w -> p k (g w)")
                tx = shift[:, t, 0:1].rearrange("p k g w -> p k (g w)").broadcast_to([P, 2, G * WP])
                ty = shift[:, t, 1].rearrange("p g w -> p (g w)")
                dve.wait_ge(v_corner, n + 1)
                dve.wait_ge(v_centre, n + 1)
                nc.vector.tensor_tensor(pair, pair, base, ALU.subtract).then_inc(v_xdiff, 1)
                if not (fresh and u < LAG):
                    result(b, i, u - LAG)
                dve.wait_ge(v_xdiff, n + 1)
                dve.wait_ge(size_done[0], n + 1)
                nc.vector.tensor_tensor(pair, tx, pair, ALU.mult).then_inc(v_xprod, 1)
                dve.wait_ge(v_xprod, n + 1)
                nc.vector.tensor_tensor(pair, base, pair, ALU.add).then_inc(v_xlerp, 1)
                chosen, middle = (near[:, t, k].rearrange("p g w -> p (g w)") for k in range(2))
                dve.wait_ge(v_xlerp, n + 1)
                nc.vector.tensor_tensor(chosen, chosen, middle, ALU.subtract).then_inc(v_ydiff, 1)
                dve.wait_ge(v_ydiff, n + 1)
                dve.wait_ge(size_done[1], n + 1)
                nc.vector.tensor_tensor(chosen, ty, chosen, ALU.mult).then_inc(v_yprod, 1)
                dve.wait_ge(v_yprod, n + 1)
                dve.wait_ge(moved[z], (uses(b, i, u - 3, NU) + 1) * MOVED)
                dve.wait_ge(moved[(z + 1) % NU], (uses(b, i, u - 2, NU) + 1) * MOVED)
                dve.wait_ge(dn_last[(z - 1) % NU], (uses(b, i, u - 4, NU) + 1) * LAST)
                nc.vector.tensor_tensor(samp[:, z].rearrange("p g w -> p (g w)"), middle, chosen, ALU.add).then_inc(samp_done, 1)

            def step(b, i, u, s, fresh):
                m = i * U + u
                n = b * STEPS + m
                if s == STEPS - 3:
                    deviation(b + 2)
                if s == STEPS - 2:
                    variance(b + 2)
                sample(b, i, u, fresh)
                if s == STEPS - 2:
                    coefficients(b + 2)
                if s == STEPS - 4:
                    partition_stats(b + 2)

            images(dve, step)
            for late in range(U - LAG, U):
                result(B - 1, ITERS - 1, late)


def kernel(x, L0_conv_w_off, L0_conv_b_off, L0_conv_w_dcn, L0_conv_b_dcn):
    import numpy as np
    import concourse.bacc as bacc
    from concourse.bass_utils import run_bass_kernel_spmd

    x, w_off, b_off, w_dcn, b_dcn = (np.ascontiguousarray(a) for a in (
        x, L0_conv_w_off, L0_conv_b_off, L0_conv_w_dcn, L0_conv_b_dcn))
    w_all = np.stack([w_off[0::2], w_off[1::2], w_dcn])
    w_all = np.ascontiguousarray(w_all.transpose(3, 0, 4, 2, 1))
    bias_all = np.ascontiguousarray(np.stack([b_off[0::2], b_off[1::2], b_dcn], axis=1))
    source = np.arange(P) // BANDS // GROUP
    target = np.arange(P) % C // GROUP
    share = np.float32(1 / (GROUP * BANDS))
    avg_src = np.where(source[:, None] == source[None, :], share, np.float32(0))
    avg_dst = np.where(source[:, None] == target[None, :], share, np.float32(0))

    nc = bacc.Bacc("TRN2", target_bir_lowering=False, num_devices=1)
    arrays = {"x": x, "w_all": w_all, "bias_all": bias_all, "avg_src": avg_src, "avg_dst": avg_dst}
    args = [nc.dram_tensor(f"in_{k}", a.shape, mybir.dt.from_np(a.dtype), kind="ExternalInput").ap()
            for k, a in arrays.items()]
    out = nc.dram_tensor("out", x.shape, mybir.dt.float32, kind="ExternalOutput").ap()
    conv_kernel(nc, *args, out)
    r = run_bass_kernel_spmd(nc, [{f"in_{k}": a for k, a in arrays.items()}], core_ids=[0])
    return r.results[0]["out"]
```

```python
from contextlib import ExitStack

import concourse.bass as bass
from concourse import mybir

B, C, H, W = 8, 32, 384, 384
KW = 3
GROUP = 2
EPS = 1e-5

QR = 4
P = QR * C
G = 2
SR = G * QR
STEPS = H // SR
U = 6
ITERS = STEPS // U
WP = W + 2
HALF = P // 2

AHEAD = 3
NX, NN, NT, NU, NO = 6, 3, 2, 3, 2
LAG = 3
CREDIT = 6

BANDS = P // C
SPAN = H * W // BANDS
CHUNKS = (ITERS - 2) * U
CH = SPAN // CHUNKS
NS = 2
NF = 6
assert CHUNKS * CH == SPAN and STEPS % U == 0 and CHUNKS % NS == 0

OX, OY, OUTC = 0, 1, 2
CONSTS = 2 * KW + QR + 2
INNER, TOP, BOTTOM = 0, 1, 2


def conv_kernel(nc, x, w_all, bias_all, avg_src, avg_dst, out):
    f32 = mybir.dt.float32
    u32 = mybir.dt.uint32
    ALU = mybir.AluOpType
    ACT = mybir.ActivationFunctionType

    def image(t, b):
        return t[bass.ds(b, 1), :, :, :].rearrange("b c h w -> (b c) h w")

    def own_rows(t, b, row0):
        return image(t, b)[:, bass.ds(row0, G, QR), :]

    def image_rows(b, row0, n):
        return image(x, b)[:, bass.ds(row0, n), :]

    def windows(b, row0):
        v = image(x, b)[:, bass.ds(row0 - 1, G, QR), :]
        return bass.AP(tensor=v.tensor, offset=v.offset, ap=[*v.ap[:-1], [1, 3 * W]])

    def chunks(b, q):
        v = x[bass.ds(b, 1), :, :, :].rearrange("b c (q r) w -> (b c q) (r w)", q=BANDS)
        return v[:, bass.ds(q * CH, CH)]

    ctx = ExitStack()
    with ctx:
        def sb(name, shape, dt=f32):
            return ctx.enter_context(nc.sbuf_tensor(name, shape, dt))

        def ps(name, shape):
            return ctx.enter_context(nc.psum_tensor(name, shape, f32))

        def sem(name):
            return ctx.enter_context(nc.semaphore(name))

        x_in = sb("x_in", [P, NX, G, 3, W])
        CENTRE, UP, MID, DOWN = 0, 1, 2, 3
        norm = sb("norm", [P, NN, 4, G, WP])
        near = sb("near", [P, NT, 3, G, WP])
        shift = sb("shift", [P, NT, 2, G, WP])
        pick = sb("pick", [P, NT, 2, G, WP])
        samp = sb("samp", [P, NU, G, WP])
        samp_up = sb("samp_up", [P, NU, G, WP])
        samp_dn = sb("samp_dn", [P, NU, G, WP])
        res = sb("res", [P, NO, G, W])
        stat_in = sb("stat_in", [P, NS, CH])
        stat_out = sb("stat_out", [P, CH])
        chunk_sum = sb("chunk_sum", [P, NS])
        neg_mean = sb("neg_mean", [P, CHUNKS])
        sq_dev = sb("sq_dev", [P, CHUNKS])
        bn_mean = sb("bn_mean", [P, 6])
        agg = sb("agg", [P, 3])
        mv = sb("mv", [P, 2])
        dev = sb("dev", [P, 4])
        gvar = sb("gvar", [P, 1])
        coef_next = sb("coef_next", [P, 2])
        minus_half = sb("minus_half", [P, 1])
        coef = sb("coef", [P, 2])
        wt = sb("wt", [P, 3, 3, KW, HALF])
        bias = sb("bias", [P, 3])
        a_src = sb("a_src", [P, P])
        a_dst = sb("a_dst", [P, P])

        p_off = [ps(f"p_off{k}", [P, G, 512]) for k in range(2)]
        p_out = ps("p_out", [P, G, 512])
        p_stat = ps("p_stat", [P, 512])

        consts_in = sem("consts_in")
        zeroed = sem("zeroed")
        weights_seq = sem("weights_seq")
        var_ready = sem("var_ready")
        root_done = sem("root_done")
        weights_ready = sem("weights_ready")
        tiles_ready = sem("tiles_ready")
        pads_ready = sem("pads_ready")
        rows_in = [sem(f"rows_in_{k}") for k in range(AHEAD)]
        top_in = sem("top_in")
        bottom_in = sem("bottom_in")
        moved = [sem(f"moved_{k}") for k in range(NU)]
        dn_last = [sem(f"dn_last_{k}") for k in range(NU)]
        stored = [sem("stored_even"), sem("stored_odd")]
        first_got = [sem(f"first_got_{k}") for k in range(NF)]
        stat_got = [sem("stat_got_0"), sem("stat_got_1")]
        sum_done = sem("sum_done")
        mean_done = sem("mean_done")
        stat_seq = sem("stat_seq")
        agg_seq = sem("agg_seq")
        stat_agg = sem("stat_agg")
        mean_mm = sem("mean_mm")
        dev_seq = sem("dev_seq")
        group_mm = sem("group_mm")
        coef_ready = sem("coef_ready")
        coef_set = sem("coef_set")
        norm_done = sem("norm_done")
        left_done = sem("left_done")
        upper_done = sem("upper_done")
        off_mm = [sem("xoff_mm"), sem("yoff_mm")]
        tanh_done = [sem("xtanh_done"), sem("ytanh_done")]
        size_done = sem("size_done")
        pick_done = [sem("xpick_done"), sem("ypick_done")]
        v_near = sem("v_near")
        v_centre = sem("v_centre")
        v_corner = sem("v_corner")
        v_xdiff = sem("v_xdiff")
        v_xprod = sem("v_xprod")
        v_xlerp = sem("v_xlerp")
        v_ydiff = sem("v_ydiff")
        v_yprod = sem("v_yprod")
        samp_done = sem("samp_done")
        out_mm = sem("out_mm")
        out_done = sem("out_done")

        held = {"sp": sem("sp_held"), "dve": sem("dve_held")}

        def hold(eng, name, semaphore, value):
            eng.wait_ge(semaphore, value)
            eng.sem_inc(held[name], 1)

        block = ctx.enter_context(nc.Block())

        def flat(planes):
            return planes.rearrange("p k g w -> p k (g w)")

        def line(plane):
            return plane.rearrange("p g w -> p (g w)")

        ROWS_IN, EDGE_IN, MOVED, LAST, STORED = QR * 16, 2 * 16, 5 * 16, 16, QR * 16

        def uses(b, i, u, ring):
            return b * (STEPS // ring) + i * (U // ring) + u // ring + 1

        def images(eng, step):
            def one(b, fresh):
                for u in range(U):
                    step(b, 0, u, u, fresh)
                with eng.Fori(1, ITERS - 1) as i:
                    for u in range(U):
                        step(b, i, u, None, False)
                for u in range(U):
                    step(b, ITERS - 1, u, STEPS - U + u, False)

            one(0, True)
            with eng.Fori(1, B) as b:
                one(b, False)

        def first_chunk(q):
            k = q % NF
            return x_in[:, NX - NF // 2 + k // 2].rearrange("p g k w -> p (g k w)")[:, k % 2 * CH:(k % 2 + 1) * CH]

        def stat_load(eng, b, q, slot):
            eng.dma_start(stat_in[:, slot, :], chunks(b, q)).then_inc(stat_got[slot], 16)

        @block.sync
        def _(sp):
            def load(b, row0, slot, first, last):
                landed = rows_in[slot % AHEAD]
                for r in range(QR):
                    dst = x_in[r * C:(r + 1) * C, slot]
                    if first and r == 0:
                        sp.dma_start(dst[:, 1], image_rows(b, QR - 1, 3)).then_inc(landed, 16)
                        sp.dma_start(dst[:, 0, 1:3], image_rows(b, 0, 2)).then_inc(top_in, 16)
                        sp.dma_start(dst[:, 0, 0:1], image_rows(b, 1, 1)).then_inc(top_in, 16)
                    elif last and r == QR - 1:
                        sp.dma_start(dst[:, 0], image_rows(b, H - QR - 2, 3)).then_inc(landed, 16)
                        sp.dma_start(dst[:, 1, 0:2], image_rows(b, H - 2, 2)).then_inc(bottom_in, 16)
                        sp.dma_start(dst[:, 1, 2:3], image_rows(b, H - 2, 1)).then_inc(bottom_in, 16)
                    else:
                        sp.dma_start(dst.rearrange("c g k w -> c g (k w)"), windows(b, row0 + r)).then_inc(landed, 16)

            for q in range(CHUNKS):
                if q >= NF:
                    sp.wait_ge(stat_seq, q - NF + 1)
                sp.dma_start(first_chunk(q), chunks(0, q)).then_inc(first_got[q % NF], 16)
            sp.wait_ge(zeroed, 1)
            for ro in range(2):
                for ky in range(KW):
                    kr = ro + ky
                    sp.dma_start(
                        wt[kr * C:(kr + 1) * C, INNER, :, :, ro * C:(ro + 1) * C].rearrange("k u d m -> k (u d) m"),
                        w_all[ky].rearrange("u d k m -> k (u d) m")).then_inc(consts_in, 16)
            for r in range(QR):
                sp.dma_start(bias[r * C:(r + 1) * C, :], bias_all).then_inc(consts_in, 16)
            sp.dma_start(a_src[:, :], avg_src).then_inc(consts_in, 16)
            sp.dma_start(a_dst[:, :], avg_dst).then_inc(consts_in, 16)
            for s in range(AHEAD):
                load(0, s * SR, s, s == 0, False)

            def step(b, i, u, s, fresh):
                m = i * U + u
                n = b * STEPS + m
                nxt = (b + 1) % B
                hold(sp, "sp", out_done, n + AHEAD - NX + 1 + CREDIT)
                hold(sp, "sp", norm_done, n + 1)
                over = s is not None and s >= STEPS - AHEAD
                bb, row = (nxt, (s + AHEAD - STEPS) * SR) if over else (b, (m + AHEAD) * SR)
                load(bb, row, (u + AHEAD) % NX, over and row == 0, s == STEPS - 1 - AHEAD)
                if not (fresh and s < LAG):
                    before = s is not None and s < LAG
                    store(n - LAG, b - 1 if before else b, (STEPS + s - LAG if before else m - LAG) * SR, u - LAG)
                hold(sp, "sp", samp_done, n + 1 + CREDIT)
                hold(sp, "sp", out_mm, n - LAG + 1 + CREDIT)
                a, z = u % NU, (u - 1) % NU
                sp.dma_start(samp_up[C:P, a], samp[0:P - C, a]).then_inc(moved[a], 16)
                sp.dma_start(samp_up[0:C, a, 1:G], samp[P - C:P, a, 0:G - 1]).then_inc(moved[a], 16)
                above = samp[P - C:P, a, G - 1] if s == 0 else samp[P - C:P, z, G - 1]
                if s == 0:
                    above = samp[0:C, a, 0]
                sp.dma_start(samp_up[0:C, a, 0], above).then_inc(moved[a], 16)
                sp.dma_start(samp_dn[0:P - C, a], samp[C:P, a]).then_inc(moved[a], 16)
                sp.dma_start(samp_dn[P - C:P, a, 0:G - 1], samp[0:C, a, 1:G]).then_inc(moved[a], 16)
                if s != 0:
                    sp.dma_start(samp_dn[P - C:P, z, G - 1], samp[0:C, a, 0]).then_inc(dn_last[z], 16)
                if s == STEPS - 1:
                    sp.dma_start(samp_dn[P - C:P, a, G - 1], samp[0:C, a, 0]).then_inc(dn_last[a], 16)


            def store(n, b, row0, u):
                hold(sp, "sp", out_done, n + 1 + CREDIT)
                for r in range(QR):
                    sp.dma_start(own_rows(out, b, row0 + r), res[r * C:(r + 1) * C, u % NO]).then_inc(stored[u % NO], 16)

            for k in range(NU):
                sp.sem_inc(moved[k], MOVED)
                sp.sem_inc(dn_last[k], LAST)
            for k in range(NO):
                sp.sem_inc(stored[k], STORED)
            images(sp, step)
            for late in range(LAG):
                s = STEPS - LAG + late
                store((B - 1) * STEPS + s, B - 1, s * SR, s)
            for k in range(2):
                sp.wait_ge(stored[k], (B * STEPS // 2 + 1) * STORED)
            for k in range(AHEAD):
                sp.wait_ge(rows_in[k], (B * STEPS // AHEAD + 1) * ROWS_IN)

        @block.gpsimd
        def _(pool):
            for t in (samp_up, samp_dn, samp):
                nc.gpsimd.memset(t[:], 0.0).then_inc(tiles_ready, 1)
            for t in (norm, near, shift):
                nc.gpsimd.memset(t[:], 0.0).then_inc(pads_ready, 1)
            nc.gpsimd.memset(pick[:], 0.0).then_inc(pads_ready, 1)
            pool.wait_ge(pads_ready, 4)
            nc.gpsimd.memset(pick[:, :, 0, :, 1:2], 1.0).then_inc(pads_ready, 1)
            nc.gpsimd.memset(minus_half[:], -0.5).then_inc(pads_ready, 1)
            pool.wait_ge(pads_ready, 6)

            def root(images):
                pool.wait_ge(var_ready, images)
                nc.gpsimd.tensor_tensor(coef_next[:, 0:1], gvar[:, :], minus_half[:, :], ALU.pow).then_inc(root_done, 1)

            root(1)
            with pool.Fori(0, B) as b:
                root(b + 2)

        @block.scalar
        def _(act):

            def normalise(b, i, u, s):
                n, a = b * STEPS + i * U + u, u % NN
                act.wait_ge(rows_in[u % AHEAD], uses(b, i, u, AHEAD) * ROWS_IN)
                if s is not None and s % STEPS == 0:
                    act.wait_ge(top_in, (b + 1 + s // STEPS) * EDGE_IN)
                if s == STEPS - 1:
                    act.wait_ge(bottom_in, (b + 1) * EDGE_IN)
                act.wait_ge(samp_done, n - 2 + CREDIT)
                act.wait_ge(off_mm[1], n - 2 + CREDIT)
                nc.scalar.activation(norm[:, a, UP:DOWN + 1, :, 1:W + 1], x_in[:, u % NX].rearrange("p g k w -> p k g w"),
                                     ACT.Identity, bias=coef[:, 1:2], scale=coef[:, 0:1]).then_inc(norm_done, 1)

            def lay_upper(n, u):
                a = u % NN
                act.wait_ge(norm_done, n + 1)
                nc.scalar.activation(norm[:, a, CENTRE, :, 1:W + 1], norm[:, a, UP, :, 1:W + 1],
                                     ACT.Copy).then_inc(upper_done, 1)

            def lay_left(n, u):
                a, t = u % NN, u % NT
                act.wait_ge(norm_done, n + 1)
                act.wait_ge(samp_done, n - 1 + CREDIT)
                nc.scalar.activation(flat(near[:, t])[:, :, 1:G * WP],
                                     flat(norm[:, a, UP:DOWN + 1])[:, :, 0:G * WP - 1], ACT.Copy).then_inc(left_done, 1)

            def new_coefficients(images):
                act.wait_ge(coef_ready, images)
                act.wait_ge(norm_done, (images - 1) * STEPS)
                nc.scalar.activation(coef[:, :], coef_next[:, :], ACT.Copy).then_inc(coef_set, 1)
                act.wait_ge(coef_set, images)

            def chunk_stats(images, q, slot, n_got):
                act.wait_ge(stat_got[slot], n_got * 16)
                act.wait_ge(stat_seq, images * CHUNKS + q)
                nc.scalar.activation(stat_out[:, :], stat_in[:, slot, :], ACT.Copy,
                                     accum_out=chunk_sum[:, slot:slot + 1]).then_inc(sum_done, 1)
                act.wait_ge(sum_done, images * CHUNKS + q + 1)
                mean = neg_mean[:, bass.ds(q, 1)]
                nc.scalar.activation(neg_mean[:, bass.ds(q, 1)], chunk_sum[:, slot:slot + 1], ACT.Copy,
                                     scale=-1.0 / CH).then_inc(mean_done, 1)
                act.wait_ge(mean_done, images * CHUNKS + q + 1)
                nc.scalar.activation(stat_out[:, :], stat_in[:, slot, :], ACT.Square, bias=mean,
                                     accum_out=sq_dev[:, bass.ds(q, 1)]).then_inc(stat_seq, 1)

            for q in range(CHUNKS):
                act.wait_ge(mean_done, q + 1)
                if q:
                    act.wait_ge(stat_seq, q)
                nc.scalar.activation(stat_out[:, :], first_chunk(q), ACT.Square, bias=neg_mean[:, q:q + 1],
                                     accum_out=sq_dev[:, q:q + 1]).then_inc(stat_seq, 1)
            act.wait_ge(pads_ready, 6)
            act.wait_ge(weights_ready, 2)
            act.sem_inc(tanh_done[0], CREDIT)
            act.sem_inc(tanh_done[1], CREDIT)
            act.wait_ge(coef_ready, 1)
            nc.scalar.activation(coef[:, :], coef_next[:, :], ACT.Copy).then_inc(coef_set, 1)
            act.wait_ge(coef_set, 1)
            normalise(0, 0, 0, 0)
            lay_upper(0, 0)
            lay_left(0, 0)

            def step(b, i, u, s, fresh):
                m = i * U + u
                n = b * STEPS + m
                t = u % NT
                if s is None:
                    q = (i - 1) * U + u
                    act.wait_ge(stat_seq, (b + 1) * CHUNKS + q - NS + 1)
                    stat_load(act, (b + 1) % B, q, u % NS)
                act.wait_ge(samp_done, n - 1 + CREDIT)
                for k in range(2):
                    lo, hi = (1, W - 1) if k == 0 else (0, W)
                    act.wait_ge(off_mm[k], n + 1 + CREDIT)
                    nc.scalar.activation(pick[:, t, k, :, 1 + lo:1 + hi], p_off[k][:, :, lo:hi], ACT.Relu,
                                         bias=bias[:, k:k + 1], scale=-0.5).then_inc(pick_done[k], 1)
                    nc.scalar.activation(shift[:, t, k, :, 1:W + 1], p_off[k][:, :, 0:W], ACT.Tanh,
                                         bias=bias[:, k:k + 1], scale=-0.5).then_inc(tanh_done[k], 1)
                    if k == 0:
                        if s == STEPS - 1:
                            new_coefficients(b + 2)
                        normalise(b, i, u + 1, None if s is None else s + 1)
                act.wait_ge(tanh_done[0], n + 1 + CREDIT)
                act.wait_ge(tanh_done[1], n + 1 + CREDIT)
                nc.scalar.activation(flat(shift[:, t]), flat(shift[:, t]), ACT.Abs, scale=0.5).then_inc(size_done, 1)
                lay_upper(n + 1, u + 1)
                if s is None:
                    chunk_stats(b + 1, q, u % NS, b * (CHUNKS // NS) + (i - 1) * (U // NS) + u // NS + 1)
                lay_left(n + 1, u + 1)

            images(act, step)

        @block.tensor
        def _(pe):
            pe.wait_ge(consts_in, 16 * CONSTS)
            pe.sem_inc(off_mm[0], CREDIT)
            pe.sem_inc(off_mm[1], CREDIT)
            pe.sem_inc(out_mm, CREDIT)

            def group_mean():
                nc.tensor.matmul(p_stat[:, 0:1], a_src[:, :], mv[:, 0:1], start=True, stop=True).then_inc(mean_mm, 1)

            def group_both():
                nc.tensor.matmul(p_stat[:, 2:4], a_dst[:, :], dev[:, 2:4], start=True, stop=True).then_inc(group_mm, 1)

            pe.wait_ge(stat_agg, 1)
            pe.wait_ge(agg_seq, 4)
            group_mean()
            pe.wait_ge(dev_seq, 3)
            group_both()
            pe.wait_ge(weights_ready, 2)

            def conv(dst, conv_no, above, below, first, last):
                for g in range(G):
                    for dx in range(KW):
                        for half, src in ((0, above), (1, below)):
                            v = TOP if first and g == 0 and half == 0 else \
                                BOTTOM if last and g == G - 1 and half == 1 else INNER
                            mm = nc.tensor.matmul(dst[half * HALF:(half + 1) * HALF, g, 0:W], wt[:, v, conv_no, dx, :],
                                                  src[:, g, dx:dx + W], start=(dx == 0), stop=(dx == KW - 1))
                return mm

            def offsets(n, u, first, last):
                a = u % NN
                pe.wait_ge(norm_done, n + 1)
                for k in range(2):
                    pe.wait_ge(tanh_done[k], n + CREDIT)
                    conv(p_off[k], k, norm[:, a, UP], norm[:, a, DOWN], first, last).then_inc(off_mm[k], 1)

            def output(b, i, u, first, last):
                n, a = b * STEPS + i * U + u, u % NU
                pe.wait_ge(moved[a], (uses(b, i, u, NU) + 1) * MOVED)
                pe.wait_ge(dn_last[a], (uses(b, i, u, NU) + 1) * LAST)
                pe.wait_ge(out_done, n + CREDIT)
                conv(p_out, OUTC, samp_up[:, a], samp_dn[:, a], first, last).then_inc(out_mm, 1)

            def step(b, i, u, s, fresh):
                m = i * U + u
                n = b * STEPS + m
                if s == STEPS - 2:
                    pe.wait_ge(dev_seq, (b + 2) * 3)
                    group_both()
                offsets(n, u, s == 0, s == STEPS - 1)
                if s == STEPS - 3:
                    pe.wait_ge(stat_agg, b + 2)
                    pe.wait_ge(agg_seq, (b + 2) * 4)
                    group_mean()
                if not (fresh and s < LAG):
                    output(b, i, u - LAG, s == LAG, s == LAG - 1)

            images(pe, step)
            for late in range(U - LAG, U):
                output(B - 1, ITERS - 1, late, False, late == U - 1)

        @block.vector
        def _(dve):
            nc.vector.memset(wt[:], 0.0).then_inc(zeroed, 1)
            for q in range(CHUNKS):
                dve.wait_ge(first_got[q % NF], (q // NF + 1) * 16)
                nc.vector.reduce_sum(chunk_sum[:, q % NS:q % NS + 1], first_chunk(q),
                                     axis=mybir.AxisListType.X).then_inc(sum_done, 1)
                dve.wait_ge(sum_done, q + 1)
                nc.vector.tensor_scalar(neg_mean[:, q:q + 1], chunk_sum[:, q % NS:q % NS + 1], -1.0 / CH, None,
                                        ALU.mult).then_inc(mean_done, 1)

            dve.wait_ge(consts_in, 16 * CONSTS)
            nc.vector.tensor_scalar(bias[:, 0:2], bias[:, 0:2], -0.5, None, ALU.mult).then_inc(weights_seq, 1)
            dve.wait_ge(weights_seq, 1)
            nc.vector.tensor_copy(wt[:, TOP], wt[:, INNER]).then_inc(weights_seq, 1)
            nc.vector.tensor_copy(wt[:, BOTTOM], wt[:, INNER]).then_inc(weights_seq, 1)
            dve.wait_ge(weights_seq, 3)
            nc.vector.memset(wt[0:C, TOP], 0.0).then_inc(weights_ready, 1)
            nc.vector.memset(wt[P - C:P, BOTTOM], 0.0).then_inc(weights_ready, 1)

            def partition_stats(images):
                dve.wait_ge(stat_seq, images * CHUNKS)
                nc.vector.bn_stats(bn_mean[:, :], neg_mean[:, :]).then_inc(agg_seq, 1)
                nc.vector.reduce_sum(agg[:, 2:3], sq_dev[:, :], axis=mybir.AxisListType.X).then_inc(agg_seq, 1)
                hold(dve, "dve", agg_seq, images * 4 - 2)
                nc.vector.bn_aggr(agg[:, 0:2], bn_mean[:, :]).then_inc(agg_seq, 1)
                dve.wait_ge(agg_seq, images * 4 - 1)
                nc.vector.tensor_scalar(mv[:, 0:1], agg[:, 0:1], -1.0, None, ALU.mult).then_inc(agg_seq, 1)
                nc.vector.scalar_tensor_tensor(mv[:, 1:2], agg[:, 2:3], 1.0 / SPAN, agg[:, 1:2],
                                               ALU.mult, ALU.add).then_inc(stat_agg, 1)

            def deviation(images):
                dve.wait_ge(stat_agg, images)
                dve.wait_ge(agg_seq, images * 4)
                dve.wait_ge(mean_mm, images)
                nc.vector.tensor_tensor(dev[:, 0:1], mv[:, 0:1], p_stat[:, 0:1], ALU.subtract).then_inc(dev_seq, 1)
                nc.vector.tensor_copy(dev[:, 2:3], mv[:, 0:1]).then_inc(dev_seq, 1)
                dve.wait_ge(dev_seq, images * 3 - 1)
                nc.vector.scalar_tensor_tensor(dev[:, 3:4], dev[:, 0:1], dev[:, 0:1], mv[:, 1:2],
                                               ALU.mult, ALU.add).then_inc(dev_seq, 1)

            def variance(images):
                dve.wait_ge(group_mm, images)
                nc.vector.tensor_scalar(gvar[:, :], p_stat[:, 3:4], EPS, None, ALU.add).then_inc(var_ready, 1)

            def coefficients(images):
                dve.wait_ge(root_done, images)
                nc.vector.scalar_tensor_tensor(coef_next[:, 1:2], p_stat[:, 2:3], -1.0, coef_next[:, 0:1],
                                               ALU.mult, ALU.mult).then_inc(coef_ready, 1)

            partition_stats(1)
            deviation(1)
            variance(1)
            coefficients(1)
            dve.sem_inc(samp_done, CREDIT)
            dve.sem_inc(out_done, CREDIT)

            def result(b, i, u):
                n = b * STEPS + i * U + u
                dve.wait_ge(out_mm, n + 1 + CREDIT)
                dve.wait_ge(stored[u % NO], (uses(b, i, u - 2, NO) + 1) * STORED)
                nc.vector.scalar_tensor_tensor(res[:, u % NO], p_out[:, :, 0:W], bias[:, 2:3], x_in[:, u % NX, :, 1],
                                               ALU.add, ALU.add).then_inc(out_done, 1)

            dve.wait_ge(tiles_ready, 3)

            def y_diff(n, u):
                t = u % NT
                dve.wait_ge(v_xlerp, n + 1)
                nc.vector.tensor_tensor(line(near[:, t, 0]), line(near[:, t, 0]), line(near[:, t, 1]),
                                        ALU.subtract).then_inc(v_ydiff, 1)

            def y_prod(n, u):
                t = u % NT
                dve.wait_ge(v_ydiff, n + 1)
                nc.vector.tensor_tensor(line(near[:, t, 0]), line(shift[:, t, 1]), line(near[:, t, 0]),
                                        ALU.mult).then_inc(v_yprod, 1)

            def y_lerp(n, b, i, u):
                t, z = u % NT, u % NU
                dve.wait_ge(moved[z], (uses(b, i, u - 3, NU) + 1) * MOVED)
                dve.wait_ge(moved[(z + 1) % NU], (uses(b, i, u - 2, NU) + 1) * MOVED)
                dve.wait_ge(dn_last[(z - 1) % NU], (uses(b, i, u - 4, NU) + 1) * LAST)
                dve.wait_ge(v_yprod, n + 1)
                nc.vector.tensor_tensor(line(samp[:, z]), line(near[:, t, 1]), line(near[:, t, 0]),
                                        ALU.add).then_inc(samp_done, 1)

            def sample(b, i, u, fresh):
                n, a, t = b * STEPS + i * U + u, u % NN, u % NT
                before = not (fresh and u == 0)
                hold(dve, "dve", left_done, n + 1)
                hold(dve, "dve", pick_done[0], n + 1)
                nc.vector.copy_predicated(
                    flat(near[:, t])[:, :, 0:G * WP - 1],
                    flat(pick[:, t, 0:1]).bitcast(u32)[:, :, 0:G * WP - 1].broadcast_to([P, 3, G * WP - 1]),
                    flat(norm[:, a, UP:DOWN + 1])[:, :, 1:G * WP]).then_inc(v_near, 1)
                if before:
                    y_diff(n - 1, u - 1)
                hold(dve, "dve", upper_done, n + 1)
                hold(dve, "dve", pick_done[1], n + 1)
                nc.vector.copy_predicated(norm[:, a, CENTRE, :, 1:W + 1], pick[:, t, 1, :, 1:W + 1].bitcast(u32),
                                          norm[:, a, DOWN, :, 1:W + 1]).then_inc(v_centre, 1)
                hold(dve, "dve", v_near, n + 1)
                nc.vector.copy_predicated(near[:, t, 0, :, 1:W + 1], pick[:, t, 1, :, 1:W + 1].bitcast(u32),
                                          near[:, t, 2, :, 1:W + 1]).then_inc(v_corner, 1)
                if before:
                    y_prod(n - 1, u - 1)
                base, pair = flat(norm[:, a, CENTRE:MID + 1:MID - CENTRE]), flat(near[:, t, 0:2])
                dve.wait_ge(v_centre, n + 1)
                dve.wait_ge(v_corner, n + 1)
                nc.vector.tensor_tensor(pair, pair, base, ALU.subtract).then_inc(v_xdiff, 1)
                if before:
                    y_lerp(n - 1, b, i, u - 1)
                dve.wait_ge(size_done, n + 1)
                dve.wait_ge(v_xdiff, n + 1)
                nc.vector.tensor_tensor(pair, flat(shift[:, t, 0:1]).broadcast_to([P, 2, G * WP]), pair,
                                        ALU.mult).then_inc(v_xprod, 1)
                if not (fresh and u < LAG):
                    result(b, i, u - LAG)
                dve.wait_ge(v_xprod, n + 1)
                nc.vector.tensor_tensor(pair, base, pair, ALU.add).then_inc(v_xlerp, 1)

            def step(b, i, u, s, fresh):
                m = i * U + u
                n = b * STEPS + m
                if s == STEPS - 3:
                    deviation(b + 2)
                if s == STEPS - 2:
                    variance(b + 2)
                sample(b, i, u, fresh)
                if s == STEPS - 2:
                    coefficients(b + 2)
                if s == STEPS - 4:
                    partition_stats(b + 2)

            images(dve, step)
            last = B * STEPS - 1
            y_diff(last, U - 1)
            y_prod(last, U - 1)
            y_lerp(last, B - 1, ITERS - 1, U - 1)
            for late in range(U - LAG, U):
                result(B - 1, ITERS - 1, late)


def kernel(x, L0_conv_w_off, L0_conv_b_off, L0_conv_w_dcn, L0_conv_b_dcn):
    import numpy as np
    import concourse.bacc as bacc
    from concourse.bass_utils import run_bass_kernel_spmd

    x, w_off, b_off, w_dcn, b_dcn = (np.ascontiguousarray(a) for a in (
        x, L0_conv_w_off, L0_conv_b_off, L0_conv_w_dcn, L0_conv_b_dcn))
    w_all = np.stack([w_off[0::2], w_off[1::2], w_dcn])
    w_all = np.ascontiguousarray(w_all.transpose(3, 0, 4, 2, 1))
    bias_all = np.ascontiguousarray(np.stack([b_off[0::2], b_off[1::2], b_dcn], axis=1))
    source = np.arange(P) // BANDS // GROUP
    target = np.arange(P) % C // GROUP
    share = np.float32(1 / (GROUP * BANDS))
    avg_src = np.where(source[:, None] == source[None, :], share, np.float32(0))
    avg_dst = np.where(source[:, None] == target[None, :], share, np.float32(0))

    nc = bacc.Bacc("TRN2", target_bir_lowering=False, num_devices=1)
    arrays = {"x": x, "w_all": w_all, "bias_all": bias_all, "avg_src": avg_src, "avg_dst": avg_dst}
    args = [nc.dram_tensor(f"in_{k}", a.shape, mybir.dt.from_np(a.dtype), kind="ExternalInput").ap()
            for k, a in arrays.items()]
    out = nc.dram_tensor("out", x.shape, mybir.dt.float32, kind="ExternalOutput").ap()
    conv_kernel(nc, *args, out)
    r = run_bass_kernel_spmd(nc, [{f"in_{k}": a for k, a in arrays.items()}], core_ids=[0])
    return r.results[0]["out"]
```
